# Optimizing a Trainium2 kernel written in Bass

```python
import numpy as np
import jax
import jax.numpy as jnp

def _softmax(x, axis=-1):
    return jax.nn.softmax(x, axis=axis)

def _gelu(x):
    return jax.nn.gelu(x, approximate=True)

def _silu(x):
    return jax.nn.silu(x)

def _sigmoid(x):
    return jax.nn.sigmoid(x)

def _layernorm(x, axis=-1, eps=1e-05):
    m = jnp.mean(x, axis=axis, keepdims=True)
    v = jnp.var(x, axis=axis, keepdims=True)
    return (x - m) / jnp.sqrt(v + eps)

def _scatter_add(tgt, idx, src, axis=0):
    return tgt.at[idx].add(src)

def _segment_sum(src, seg, n):
    return jax.ops.segment_sum(src, seg, n)
kernel_name = 'mk_adj_resnorm_d1_adj_r2_083a4a'

def setup_inputs(seed: int=0):
    np.random.seed(seed)
    _w = jnp.asarray

    def _rec_inputs():
        import jax
        import jax.numpy as jnp
        _gk = jax.random.key(seed)
        x = -0.001547 + 1.001 * jax.random.normal(jax.random.fold_in(_gk, 1), (1354, 64), jnp.float32)
        _w = (1.0 + jnp.arange(1354, dtype=jnp.float32)) ** (-0.5)
        _w = _w / _w.mean()
        _pij = jnp.clip(0.0014771 * _w[:, None] * _w[None, :], 0.0, 1.0)
        _a = jax.random.uniform(jax.random.fold_in(_gk, 2), (1354, 1354)) < _pij
        _a = jnp.logical_or(_a, jnp.eye(1354, dtype=bool))
        _af = _a.astype(jnp.float32)
        _af = _af * jax.random.uniform(jax.random.fold_in(_gk, 3), (1354, 1354), jnp.float32, 0.05, 1)
        adj = _af
        return (x, adj)
    x, adj = _rec_inputs()

    def _L0_gnn_setup():
        import jax, jax.numpy as jnp
        import numpy as np

        def _laplacian(A):
            d = jnp.sum(A, axis=-1)
            dinv = 1.0 / jnp.sqrt(d)
            return A * dinv[:, None] * dinv[None, :]

        def _poly(A, theta):
            t = jax.nn.sigmoid(theta)
            N = A.shape[-1]
            P = jnp.eye(N, dtype=A.dtype)
            seg = P
            for i in range(theta.shape[0]):
                seg = seg @ A
                P = P + seg * t[i]
            return P
        key = jax.random.key(seed)
        k1, k2, k3, k4 = jax.random.split(key, 4)
        N, DIN, DOUT, K_CHEB = (2048, 64, 64, 2)
        return {'x': jax.random.normal(k1, (N, DIN), dtype=jnp.float32), 'A': jax.random.uniform(k2, (N, N), dtype=jnp.float32), 'theta': jax.random.normal(k3, (K_CHEB,), dtype=jnp.float32), 'W': jax.random.normal(k4, (DOUT, DIN), dtype=jnp.float32) / np.float32(np.sqrt(DIN)), 'b': jnp.zeros((DOUT,), dtype=jnp.float32), 'k': 4}
    _L0_gnn_all = _L0_gnn_setup()
    _L0_gnn_in = {k: v for k, v in _L0_gnn_all.items() if k in ('theta', 'W', 'b')}
    del _L0_gnn_all
    return {'x': x, 'adj': adj, 'L0_gnn_theta': _L0_gnn_in['theta'], 'L0_gnn_W': _L0_gnn_in['W'], 'L0_gnn_b': _L0_gnn_in['b']}

def reference(x, adj, L0_gnn_theta, L0_gnn_W, L0_gnn_b):
    import jax
    import jax.numpy as jnp

    def _L0_gnn_ref(x, A, theta, W, b, k):
        import jax, jax.numpy as jnp
        import numpy as np

        def _laplacian(A):
            d = jnp.sum(A, axis=-1)
            dinv = 1.0 / jnp.sqrt(d)
            return A * dinv[:, None] * dinv[None, :]

        def _poly(A, theta):
            t = jax.nn.sigmoid(theta)
            N = A.shape[-1]
            P = jnp.eye(N, dtype=A.dtype)
            seg = P
            for i in range(theta.shape[0]):
                seg = seg @ A
                P = P + seg * t[i]
            return P
        S = _laplacian(A)
        S = _poly(S, theta)
        S = _laplacian(S)
        rank = jnp.argsort(jnp.argsort(-S, axis=-1), axis=-1)
        mask = jnp.where(rank < k, jnp.float32(1.0), jnp.float32(0.0))
        S = S * mask
        x = S @ x
        return x @ W.T + b
    x = _layernorm(x + _L0_gnn_ref(x, adj, L0_gnn_theta, L0_gnn_W, L0_gnn_b, 4), axis=-1)
    return x

_drawn_inputs = setup_inputs


def setup_inputs(seed=0):
    import zlib

    import numpy as np

    out = dict(_drawn_inputs(seed))
    spreads = {'L0_gnn_b': (0.0, 0.1)}
    factors = {'L0_gnn_theta': 64.0}
    for name, (base, spread) in spreads.items():
        noise = np.random.default_rng([zlib.crc32(name.encode()), seed]).standard_normal(out[name].shape)
        drawn = base * np.exp(spread * noise) if base else spread * noise
        out[name] = jnp.asarray(drawn.astype(out[name].dtype))
    for name, factor in factors.items():
        out[name] = (out[name] * factor).astype(out[name].dtype)
    return out
```

```python
import concourse.bass as bass
import concourse.mybir as mybir
from contextlib import ExitStack


def program(nc, x, adj, adj_t, x_t, w_t, theta, bias, out):
    f32, f32r, u32 = mybir.dt.float32, mybir.dt.float32r, mybir.dt.uint32
    ALU = mybir.AluOpType
    ACT = mybir.ActivationFunctionType

    N, C = x.shape
    TOP = 4
    EPS = 1e-5
    T = (N + 127) // 128
    LAST = N - 128 * (T - 1)
    NPAD = 128 * T
    BANK = 512
    CHUNKS = [(c, min(BANK, N - c)) for c in range(0, N, BANK)]
    SET = BANK * len(CHUNKS)
    RING = 4
    QS = 4
    GS = 4

    def rows(t):
        return 128 if t < T - 1 else LAST

    with ExitStack() as ctx:
        def sb(name, shape, dt=f32):
            return ctx.enter_context(nc.sbuf_tensor(name, shape, dt))

        def sem(name):
            return ctx.enter_context(nc.semaphore(name))

        b_hi = sb("b_hi", [128, T, N], f32r)
        b_lo = sb("b_lo", [128, T, N], f32r)
        at_raw = sb("at_raw", [128, 2, T, 128])
        at_hi = sb("at_hi", [128, 2, T, 128], f32r)
        at_lo = sb("at_lo", [128, 2, T, 128], f32r)
        a_ring = sb("a_ring", [128, RING, N])
        q = sb("q", [128, QS, N])
        row_vec = sb("row_vec", [128, N])
        ident = sb("ident", [128, 128])
        t0_ident = sb("t0_ident", [128, 128])
        diag = sb("diag", [128, 128])
        h = sb("h", [128, T, C])
        picked = sb("picked", [128, GS, TOP, C])
        top = sb("top", [128, T, 8])
        top_at = sb("top_at", [128, T, 8], u32)
        coef = sb("coef", [128, T, TOP])
        t_gate = sb("t_gate", [128, 2])
        rowsum = sb("rowsum", [128, T])
        rinv = sb("rinv", [128, T])
        b_scale = sb("b_scale", [128, T])
        d = sb("d", [128, T])
        dot = sb("dot", [128, T])
        u = sb("u", [128, T])
        deg2 = sb("deg2", [128, T])
        e = sb("e", [128, T])
        work = sb("work", [128, 4, T])
        to_rows = sb("to_rows", [128, 32])
        in_rows = sb("in_rows", [128, 32])
        stats = sb("stats", [128, 6])
        mean_var = sb("mean_var", [128, T, 2])
        rstd = sb("rstd", [128, 3, T])

        xt_sb = q[0:C, 0, :]
        wt_sb = q[0:C, 1, 0:C]
        bias_sb = q[:, 1, C:2 * C]
        th_sb = q[:, 1, 2 * C:2 * C + 2]
        y_sb = q[:, 3, 0:T * C]

        ps = ctx.enter_context(nc.psum_tensor("ps", [128, 8 * BANK], f32))
        y_ps = ps[:, 2 * SET:2 * SET + T * C]

        y_dram = nc.dram_tensor("y_dram", [N, C], f32, kind="Internal").ap()
        vec_dram = [nc.dram_tensor(f"vec{i}_dram", [NPAD], f32, kind="Internal").ap() for i in range(3)]

        a_in = [sem(f"a_in{i}") for i in range(RING)]
        at0_in = [sem(f"at0_in{k}") for k in range(T)]
        at_in = [sem(f"at_in{i}") for i in range(2)]
        th_in, bias_in, x_in, xw_in = sem("th_in"), sem("bias_in"), sem("x_in"), sem("xw_in")
        y_mm, y_copied, y_out = sem("y_mm"), sem("y_copied"), sem("y_out")
        gate_ready, cleared, ident_ready, t0_ready, h_init = (
            sem("gate_ready"), sem("cleared"), sem("ident_ready"), sem("t0_ready"), sem("h_init"))
        rs_ready, rinv_ready, scale_ready = sem("rs_ready"), sem("rinv_ready"), sem("scale_ready")
        bh_full, bl_full, diag_sum, diag_hi, b_ready = (
            sem("bh_full"), sem("bl_full"), sem("diag_sum"), sem("diag_hi"), sem("b_ready"))
        ah_ready, al_ready = sem("ah_ready"), sem("al_ready")
        hi_ready, lo_ready = sem("hi_ready"), sem("lo_ready")
        sqrt_ready, newton, vec_ready, turned, vec_out, vec_in = (
            sem("sqrt_ready"), sem("newton"), sem("vec_ready"), sem("turned"), sem("vec_out"), sem("vec_in"))
        a_used, dots_done = sem("a_used"), sem("dots_done")
        tile_done, evacuated = sem("tile_done"), sem("evacuated")
        scaled, diag_added, maxed, ranked, coef_ready = (
            sem("scaled"), sem("diag_added"), sem("maxed"), sem("ranked"), sem("coef_ready"))
        gathered = [sem(f"gathered{i}") for i in range(GS)]
        mixed, summed, h_stats, h_moments = sem("mixed"), sem("summed"), sem("h_stats"), sem("h_moments")
        ve_ready, vr_ready, rstd_ready, normed, stored = (
            sem("ve_ready"), sem("vr_ready"), sem("rstd_ready"), sem("normed"), sem("stored"))

        block = ctx.enter_context(nc.Block())

        def slot(n):
            return a_ring[:, n % RING, :]

        @block.sync
        def _(sp):
            def load_a(n):
                k = n % T
                if n >= RING:
                    sp.wait_ge(a_used, n - RING + 1)
                sp.dma_start(a_ring[0:rows(k), n % RING, :],
                             adj[k * 128:k * 128 + rows(k), :]).then_inc(a_in[n % RING], 16)

            def load_at(m):
                sp.wait_ge(ah_ready, T)
                sp.wait_ge(al_ready, T)
                if m >= 4:
                    sp.wait_ge(hi_ready, m - 3)
                    sp.wait_ge(lo_ready, m - 3)
                w = rows(m)
                sp.dma_start(at_raw[:, m % 2, 0:T - 1, 0:w],
                             adj_t[0:(T - 1) * 128, m * 128:m * 128 + w].rearrange("(k p) i -> p k i", p=128)
                             ).then_inc(at_in[m % 2], 16)
                sp.dma_start(at_raw[0:LAST, m % 2, T - 1, 0:w],
                             adj_t[(T - 1) * 128:N, m * 128:m * 128 + w]).then_inc(at_in[m % 2], 16)

            def spread(i):
                sp.wait_ge(turned, i + 1)
                for g in range(4):
                    sp.dma_start(vec_dram[i].rearrange("(t g c) -> g t c", g=4, c=32)[g],
                                 in_rows[32 * g:32 * g + T, :]).then_inc(vec_out, 16)
                sp.wait_ge(vec_out, 64 * (i + 1))
                if i:
                    sp.wait_ge(dots_done, i)
                sp.dma_start(row_vec[:, :], vec_dram[i][0:N].partition_broadcast(128)).then_inc(vec_in, 16)

            for k in range(T):
                load_a(k)
                sp.dma_start(at_raw[0:rows(k), :, k, :],
                             adj_t[k * 128:k * 128 + rows(k), 0:256].rearrange("p (b i) -> p b i", b=2)
                             ).then_inc(at0_in[k], 16)
            spread(0)
            for n in range(T, T + RING):
                load_a(n)
            load_at(2)
            load_at(3)
            for n in range(T + RING, 2 * T):
                load_a(n)
            load_at(4)
            load_at(5)
            spread(1)
            for n in range(2 * T, 3 * T):
                load_a(n)
            spread(2)
            for m in range(6, T):
                load_at(m)
            sp.wait_ge(normed, T - 1)
            sp.dma_start(out[0:(T - 1) * 128, :].rearrange("(t p) c -> p t c", p=128),
                         h[:, 0:T - 1, :]).then_inc(stored, 16)
            sp.wait_ge(normed, T)
            sp.dma_start(out[(T - 1) * 128:N, :], h[0:LAST, T - 1, :]).then_inc(stored, 16)
            sp.wait_ge(stored, 32)

        @block.scalar
        def _(act):
            act.dma_start(th_sb, theta.partition_broadcast(128)).then_inc(th_in, 16)
            act.dma_start(xt_sb, x_t).then_inc(xw_in, 16)
            act.dma_start(wt_sb, w_t).then_inc(xw_in, 16)
            act.dma_start(bias_sb, bias.partition_broadcast(128)).then_inc(bias_in, 16)
            act.dma_start(h[:, 0:T - 1, :], x[0:(T - 1) * 128, :].rearrange("(t p) c -> p t c", p=128)
                          ).then_inc(x_in, 16)
            act.dma_start(h[0:LAST, T - 1, :], x[(T - 1) * 128:N, :]).then_inc(x_in, 16)
            act.wait_ge(th_in, 16)
            nc.scalar.activation(t_gate[:, :], th_sb, ACT.Sigmoid).then_inc(gate_ready, 1)

            def row_sum(k):
                p = rows(k)
                if k == 0:
                    act.wait_ge(cleared, 1)
                act.wait_ge(a_in[k % RING], 16 * (k // RING + 1))
                nc.scalar.activation(b_hi[0:p, k, :], a_ring[0:p, k % RING, :], ACT.Copy,
                                     accum_out=rowsum[0:p, k:k + 1]).then_inc(rs_ready, 1)

            row_sum(0)
            for k in range(T):
                p = rows(k)
                if k + 1 < T:
                    row_sum(k + 1)
                act.wait_ge(scale_ready, k + 1)
                act.wait_ge(rs_ready, k + 1)
                nc.scalar.activation(b_hi[0:p, k, :], a_ring[0:p, k % RING, :], ACT.Copy,
                                     scale=b_scale[0:p, k:k + 1]).then_inc(bh_full, 1)

            def root(i):
                act.wait_ge(vec_ready, 3 * i + 1)
                nc.scalar.activation(work[:, 0, :], rinv[:, :], ACT.Sqrt).then_inc(sqrt_ready, 1)

            root(0)

            for m in range(T):
                p = rows(m)
                act.wait_ge(tile_done, m + 1)
                if m == 0:
                    act.wait_ge(newton, 4)
                if m >= QS:
                    act.wait_ge(ranked, m - QS + 1)
                if m == 1:
                    act.wait_ge(h_init, 1)
                if m == 3:
                    act.wait_ge(y_out, 32)
                nc.scalar.activation(q[0:p, m % QS, :], ps[0:p, (m % 2) * SET:(m % 2) * SET + N], ACT.Copy,
                                     scale=d[0:p, m:m + 1]).then_inc(evacuated, 1)
                if m + 2 < T:
                    w = rows(m + 2)
                    act.wait_ge(at_in[m % 2], 32 * (m // 2 + 1))
                    nc.scalar.activation(at_hi[:, m % 2, 0:T - 1, 0:w], at_raw[:, m % 2, 0:T - 1, 0:w],
                                         ACT.Copy)
                    nc.scalar.activation(at_hi[0:LAST, m % 2, T - 1, 0:w], at_raw[0:LAST, m % 2, T - 1, 0:w],
                                         ACT.Copy).then_inc(hi_ready, 1)
                if m == 3:
                    root(1)
                if m == T - 2:
                    act.wait_ge(vr_ready, 1)
                    nc.scalar.activation(rstd[:, 2, 0:T - 1], rstd[:, 1, 0:T - 1], ACT.Sqrt).then_inc(rstd_ready, 1)
            act.wait_ge(vr_ready, 2)
            nc.scalar.activation(rstd[0:LAST, 2, T - 1:T], rstd[0:LAST, 1, T - 1:T],
                                 ACT.Sqrt).then_inc(rstd_ready, 1)

        @block.tensor
        def _(pe):
            pe.wait_ge(xw_in, 32)
            for m in range(T):
                mm = nc.tensor.matmul(y_ps[0:rows(m), m * C:(m + 1) * C], xt_sb[:, m * 128:m * 128 + rows(m)],
                                      wt_sb, start=True, stop=True)
            mm.then_inc(y_mm, 1)

            def steps(b, w, k, base):
                p = rows(k)
                for n, (left, right) in enumerate(((at_hi, b_hi), (at_hi, b_lo), (at_lo, b_hi))):
                    for c, cw in CHUNKS:
                        mm = nc.tensor.matmul(ps[0:w, base + c:base + c + cw], left[0:p, b, k, 0:w],
                                              right[0:p, k, c:c + cw],
                                              start=(k == 0 and n == 0), stop=(k == T - 1 and n == 2))
                return mm

            for k in range(T):
                pe.wait_ge(b_ready, k + 1)
                pe.wait_ge(ah_ready, k + 1)
                pe.wait_ge(al_ready, k + 1)
                for m in range(2):
                    mm = steps(m, 128, k, m * SET)
                    if k == T - 1:
                        mm.then_inc(tile_done, 1)

            with pe.Fori(0, (T - 3) // 2) as i:
                for b in range(2):
                    pe.wait_ge(hi_ready, 2 * i + (b + 1))
                    pe.wait_ge(lo_ready, 2 * i + (b + 1))
                    pe.wait_ge(evacuated, 2 * i + (b + 1))
                    for k in range(T):
                        mm = steps(b, 128, k, b * SET)
                    mm.then_inc(tile_done, 1)

            pe.wait_ge(hi_ready, T - 2)
            pe.wait_ge(lo_ready, T - 2)
            pe.wait_ge(evacuated, T - 2)
            for k in range(T):
                mm = steps(0, LAST, k, 0)
            mm.then_inc(tile_done, 1)

        @block.vector
        def _(dve):
            nc.vector.memset(rowsum[:, :], 1.0).then_inc(cleared, 1)
            nc.vector.memset(dot[:, :], 1.0)
            nc.vector.memset(to_rows[:, :], 0.0).then_inc(cleared, 1)

            dve.wait_ge(gate_ready, 1)
            dve.wait_ge(ident_ready, 2)
            nc.vector.tensor_scalar(t0_ident[:, :], ident[:, :], t_gate[:, 0:1], None, ALU.mult).then_inc(t0_ready, 1)

            def scale_of(k):
                p = rows(k)
                dve.wait_ge(rs_ready, k + 1)
                nc.vector.reciprocal(rinv[0:p, k:k + 1], rowsum[0:p, k:k + 1]).then_inc(rinv_ready, 1)
                dve.wait_ge(rinv_ready, k + 1)
                nc.vector.tensor_tensor(b_scale[0:p, k:k + 1], rinv[0:p, k:k + 1], t_gate[0:p, 1:2],
                                        ALU.mult).then_inc(scale_ready, 1)

            scale_of(0)
            for k in range(T):
                p = rows(k)
                kk = slice(k * 128, k * 128 + p)
                dve.wait_ge(at0_in[k], 16)
                nc.vector.tensor_copy(at_hi[0:p, :, k, :], at_raw[0:p, :, k, :]).then_inc(ah_ready, 1)
                if k == 0:
                    dve.wait_ge(y_mm, 1)
                    nc.vector.tensor_copy(y_sb[:, 0:(T - 1) * C], y_ps[:, 0:(T - 1) * C])
                    nc.vector.tensor_copy(y_sb[0:LAST, (T - 1) * C:], y_ps[0:LAST, (T - 1) * C:]).then_inc(y_copied, 1)
                if k + 1 < T:
                    scale_of(k + 1)
                dve.wait_ge(bh_full, k + 1)
                nc.vector.scalar_tensor_tensor(b_lo[0:p, k, :], a_ring[0:p, k % RING, :], b_scale[0:p, k:k + 1],
                                               b_hi[0:p, k, :].bitcast(f32), ALU.mult, ALU.subtract).then_inc(bl_full, 1)
                if k == 0:
                    dve.wait_ge(t0_ready, 1)
                else:
                    dve.wait_ge(b_ready, k)
                nc.vector.scalar_tensor_tensor(diag[0:p, 0:p], a_ring[0:p, k % RING, kk], b_scale[0:p, k:k + 1],
                                               t0_ident[0:p, 0:p], ALU.mult, ALU.add).then_inc(a_used, 1)
                dve.wait_ge(a_used, k + 1)
                nc.vector.tensor_copy(b_hi[0:p, k, kk], diag[0:p, 0:p]).then_inc(diag_hi, 1)
                dve.wait_ge(diag_hi, k + 1)
                dve.wait_ge(bl_full, k + 1)
                nc.vector.tensor_tensor(b_lo[0:p, k, kk], diag[0:p, 0:p], b_hi[0:p, k, kk].bitcast(f32),
                                        ALU.subtract).then_inc(b_ready, 1)
            dve.wait_ge(x_in, 32)
            dve.wait_ge(bias_in, 16)
            nc.vector.tensor_tensor(h[:, 0:T - 1, :], h[:, 0:T - 1, :],
                                    bias_sb.unsqueeze(1).broadcast_to([128, T - 1, C]), ALU.add)
            nc.vector.tensor_tensor(h[0:LAST, T - 1, :], h[0:LAST, T - 1, :], bias_sb[0:LAST, :],
                                    ALU.add).then_inc(h_init, 1)

            def inverse_root(i, degree, result):
                nc.vector.reciprocal(rinv[:, :], degree).then_inc(vec_ready, 1)
                dve.wait_ge(sqrt_ready, i + 1)
                nc.vector.tensor_tensor(work[:, 1, :], work[:, 0, :], work[:, 0, :], ALU.mult).then_inc(newton, 1)
                dve.wait_ge(newton, 4 * i + 1)
                nc.vector.tensor_tensor(work[:, 2, :], work[:, 1, :], degree, ALU.mult).then_inc(newton, 1)
                dve.wait_ge(newton, 4 * i + 2)
                nc.vector.tensor_scalar(work[:, 3, :], work[:, 2, :], -0.5, 1.5, ALU.mult, ALU.add).then_inc(newton, 1)
                dve.wait_ge(newton, 4 * i + 3)
                nc.vector.tensor_tensor(result, work[:, 3, :], work[:, 0, :], ALU.mult).then_inc(newton, 1)
                dve.wait_ge(newton, 4 * i + 4)

            def turn(i, vector_copied):
                vector_copied.then_inc(vec_ready, 1)
                dve.wait_ge(vec_ready, [2, 3, 5][i])
                if i:
                    dve.wait_ge(vec_out, 64 * i)
                nc.vector.transpose(in_rows[:, :], to_rows[:, :]).then_inc(turned, 1)

            def dots(i, first):
                dve.wait_ge(vec_in, 16 * (i + 1))
                for k in range(T):
                    n = first + k
                    p = rows(k)
                    dve.wait_ge(a_in[n % RING], 16 * (n // RING + 1))
                    op = nc.vector.scalar_tensor_tensor(a_ring[0:p, n % RING, :], a_ring[0:p, n % RING, :], 1.0,
                                                        row_vec[0:p, :], ALU.mult, ALU.mult,
                                                        accum_out=dot[0:p, k:k + 1])
                    op.then_inc(a_used, 1)
                dve.wait_ge(a_used, first + T)

            dve.wait_ge(rs_ready, T)
            dve.wait_ge(scale_ready, T)
            dve.wait_ge(cleared, 2)
            inverse_root(0, rowsum[:, :], d[:, :])
            turn(0, nc.vector.tensor_copy(to_rows[:, 0:T], d[:, :]))

            dots(0, T)
            nc.vector.tensor_tensor(u[:, :], dot[:, :], rinv[:, :], ALU.mult).then_inc(dots_done, 1)
            dve.wait_ge(dots_done, 1)
            nc.vector.tensor_scalar(work[:, 1, :], u[:, :], t_gate[:, 1:2], None, ALU.mult).then_inc(summed, 1)
            dve.wait_ge(summed, 1)
            turn(1, nc.vector.scalar_tensor_tensor(to_rows[:, 0:T], d[:, :], t_gate[:, 0:1], work[:, 1, :],
                                                   ALU.mult, ALU.add))

            dots(1, 2 * T)
            nc.vector.tensor_tensor(deg2[:, :], dot[:, :], d[:, :], ALU.mult).then_inc(dots_done, 1)
            dve.wait_ge(dots_done, 2)
            nc.vector.tensor_scalar(deg2[:, :], deg2[:, :], 1.0, None, ALU.add).then_inc(summed, 1)
            dve.wait_ge(summed, 2)
            inverse_root(1, deg2[:, :], e[:, :])
            turn(2, nc.vector.tensor_tensor(to_rows[:, 0:T], d[:, :], e[:, :], ALU.mult))
            dve.wait_ge(vec_in, 48)

            def rank(m):
                p = rows(m)
                mm = slice(m * 128, m * 128 + p)
                s = q[0:p, m % QS, :]
                dve.wait_ge(evacuated, m + 1)
                nc.vector.tensor_tensor(s, s, row_vec[0:p, :], ALU.mult).then_inc(scaled, 1)
                dve.wait_ge(scaled, m + 1)
                nc.vector.scalar_tensor_tensor(q[0:p, m % QS, mm], ident[0:p, 0:p], e[0:p, m:m + 1],
                                               q[0:p, m % QS, mm], ALU.mult, ALU.add).then_inc(diag_added, 1)
                dve.wait_ge(diag_added, m + 1)
                nc.vector.max(top[0:p, m, :], s).then_inc(maxed, 1)
                dve.wait_ge(maxed, m + 1)
                nc.vector.max_index(top_at[0:p, m, :], top[0:p, m, :], s).then_inc(ranked, 1)
                nc.vector.tensor_scalar(coef[0:p, m, :], top[0:p, m, 0:TOP], e[0:p, m:m + 1], None,
                                        ALU.mult).then_inc(coef_ready, 1)

            def mix(m):
                p = rows(m)
                dve.wait_ge(gathered[m % GS], 16 * TOP * (m // GS + 1))
                dve.wait_ge(coef_ready, m + 1)
                for j in range(TOP):
                    if j:
                        dve.wait_ge(mixed, TOP * m + j)
                    nc.vector.scalar_tensor_tensor(h[0:p, m, :], picked[0:p, m % GS, j, :], coef[0:p, m, j:j + 1],
                                                   h[0:p, m, :], ALU.mult, ALU.add).then_inc(mixed, 1)
                dve.wait_ge(mixed, TOP * (m + 1))
                if m:
                    dve.wait_ge(h_moments, m)
                nc.vector.bn_stats(stats[0:p, :], h[0:p, m, :]).then_inc(h_stats, 1)
                dve.wait_ge(h_stats, m + 1)
                nc.vector.bn_aggr(mean_var[0:p, m, :], stats[0:p, :]).then_inc(h_moments, 1)

            def normalise(i, lo, hi):
                p = rows(hi - 1)
                dve.wait_ge(h_moments, hi)
                nc.vector.tensor_scalar(rstd[0:p, 0, lo:hi], mean_var[0:p, lo:hi, 1], EPS, None,
                                        ALU.add).then_inc(ve_ready, 1)
                dve.wait_ge(ve_ready, i + 1)
                nc.vector.reciprocal(rstd[0:p, 1, lo:hi], rstd[0:p, 0, lo:hi]).then_inc(vr_ready, 1)
                dve.wait_ge(rstd_ready, i + 1)
                for m in range(lo, hi):
                    nc.vector.tensor_scalar(h[0:p, m, :], h[0:p, m, :], mean_var[0:p, m, 0:1], rstd[0:p, 2, m:m + 1],
                                            ALU.subtract, ALU.mult).then_inc(normed, 1)

            for i in range((T - 1) // 2):
                rank(2 * i)
                rank(2 * i + 1)
                if i:
                    mix(2 * i - 2)
                    mix(2 * i - 1)
            mix(T - 3)
            mix(T - 2)
            normalise(0, 0, T - 1)
            rank(T - 1)
            mix(T - 1)
            normalise(1, T - 1, T)

        @block.gpsimd
        def _(pool):
            pool.memset(ident[:, :], 0.0).then_inc(ident_ready, 1)
            pool.wait_ge(ident_ready, 1)
            pool.affine_select(out=ident[:, :], in_=ident[:, :], compare_op=ALU.not_equal, fill=1.0, base=0,
                               pattern=[[-1, 128]], channel_multiplier=1).then_inc(ident_ready, 1)
            for k in range(T):
                p = rows(k)
                if k == 3:
                    pool.wait_ge(y_copied, 1)
                    pool.dma_start(y_dram[0:(T - 1) * 128, :].rearrange("(t p) c -> p t c", p=128),
                                   y_sb[:, 0:(T - 1) * C].rearrange("p (t c) -> p t c", c=C)).then_inc(y_out, 16)
                    pool.dma_start(y_dram[(T - 1) * 128:N, :], y_sb[0:LAST, (T - 1) * C:]).then_inc(y_out, 16)
                pool.wait_ge(ah_ready, k + 1)
                pool.tensor_tensor(at_lo[0:p, :, k, :], at_raw[0:p, :, k, :], at_hi[0:p, :, k, :].bitcast(f32),
                                   ALU.subtract).then_inc(al_ready, 1)

            def low_half(m):
                w = rows(m)
                b = m % 2
                pool.wait_ge(hi_ready, m - 1)
                pool.tensor_tensor(at_lo[:, b, 0:T - 1, 0:w], at_raw[:, b, 0:T - 1, 0:w],
                                   at_hi[:, b, 0:T - 1, 0:w].bitcast(f32), ALU.subtract)
                pool.tensor_tensor(at_lo[0:LAST, b, T - 1, 0:w], at_raw[0:LAST, b, T - 1, 0:w],
                                   at_hi[0:LAST, b, T - 1, 0:w].bitcast(f32), ALU.subtract).then_inc(lo_ready, 1)

            def gather(m):
                p = rows(m)
                pool.wait_ge(ranked, m + 1)
                if m == 0:
                    pool.wait_ge(y_out, 32)
                if m >= GS:
                    pool.wait_ge(mixed, TOP * (m - GS + 1))
                for j in range(TOP):
                    pool.indirect_dma_start(picked[0:p, m % GS, j, :], None, y_dram,
                                            bass.IndirectOffsetOnAxis(top_at[0:p, m, j:j + 1], 0)
                                            ).then_inc(gathered[m % GS], 16)

            for m in range(2, 6):
                low_half(m)
            for i in range((T - 1) // 2):
                low_half(i + 6)
                gather(2 * i)
                gather(2 * i + 1)
            gather(T - 1)


_SHAPE = (1354, 64)


def kernel(**inputs):
    import numpy as _np
    import concourse.bacc as _bacc
    from concourse import mybir as _mybir
    from concourse.bass_utils import run_bass_kernel_spmd as _run

    nc = _bacc.Bacc("TRN2", target_bir_lowering=False, num_devices=1)
    laid_out = {
        "x": inputs["x"], "adj": inputs["adj"], "adj_t": inputs["adj"].T, "x_t": inputs["x"].T,
        "w_t": inputs["L0_gnn_W"].T, "theta": inputs["L0_gnn_theta"], "bias": inputs["L0_gnn_b"],
    }
    arrays, args = {}, []
    for name, a in laid_out.items():
        a = _np.ascontiguousarray(a)
        arrays[f"in_{name}"] = a
        args.append(nc.dram_tensor(f"in_{name}", a.shape, _mybir.dt.from_np(a.dtype), kind="ExternalInput").ap())
    args.append(nc.dram_tensor("out_0", _SHAPE, _mybir.dt.float32, kind="ExternalOutput").ap())
    program(nc, *args)
    r = _run(nc, [arrays], core_ids=[0])
    return r.results[0]["out_0"]
```

```python
import concourse.bass as bass
import concourse.mybir as mybir
from contextlib import ExitStack


def program(nc, x, adj, adj_tail, adj_t, xw_t, theta, bias, consts, out):
    f32, f32r, u32 = mybir.dt.float32, mybir.dt.float32r, mybir.dt.uint32
    ALU = mybir.AluOpType
    ACT = mybir.ActivationFunctionType
    AX = mybir.AxisListType

    N, C = x.shape
    TOP = 4
    EPS = 1e-5
    T = (N + 127) // 128
    LAST = N - 128 * (T - 1)
    KW = T - 1
    X, Y = KW, KW + 1
    K = KW + 2
    LO_FROM = {X: 64, Y: 96}
    NPAD = 128 * T
    BANK = 512
    CHUNKS = [(c, min(BANK, N - c)) for c in range(0, N, BANK)]
    SET = BANK * len(CHUNKS)
    LAST_CHUNKS = [(N - BANK, BANK), (N - 2 * BANK, BANK), (0, N - 2 * BANK)]
    RING = 4
    LOADS = K + T + T - RING
    QS = 4
    GS = 3
    DIAGS = 128 + 2 * LAST
    HEAD = 6

    def rows(t):
        return 128 if t < T - 1 else LAST

    with ExitStack() as ctx:
        def sb(name, shape, dt=f32):
            return ctx.enter_context(nc.sbuf_tensor(name, shape, dt))

        def sem(name):
            return ctx.enter_context(nc.semaphore(name))

        b_hi = sb("b_hi", [128, K, N], f32r)
        b_lo = sb("b_lo", [128, KW, N], f32r)
        at_raw = sb("at_raw", [128, 2, K, 128])
        at_hi = sb("at_hi", [128, 2, K, 128], f32r)
        at_lo = sb("at_lo", [128, 2, KW, 128], f32r)
        a_ring = sb("a_ring", [128, RING, N])
        q = sb("q", [128, QS, N])
        row_vec = sb("row_vec", [128, N])
        const_sb = sb("const_sb", [128, DIAGS + 2])
        h = sb("h", [128, T, C])
        picked = sb("picked", [128, GS, TOP, C])
        top = sb("top", [128, T, 8])
        top_at = sb("top_at", [128, T, 8], u32)
        coef = sb("coef", [128, T, TOP])
        t_gate = sb("t_gate", [128, 2])
        rowsum = sb("rowsum", [128, K])
        rinv_k = sb("rinv_k", [128, K])
        b_scale = sb("b_scale", [128, K])
        degree = sb("degree", [128, T])
        rinv = sb("rinv", [128, T])
        d = sb("d", [128, T])
        dot = sb("dot", [128, T])
        u = sb("u", [128, T])
        deg2 = sb("deg2", [128, T])
        e = sb("e", [128, T])
        work = sb("work", [128, 4, T])
        to_rows = sb("to_rows", [128, 32])
        in_rows = sb("in_rows", [128, 32])
        stats = sb("stats", [128, 6])
        mean_var = sb("mean_var", [128, T, 2])
        eps = sb("eps", [128, 1])
        std = sb("std", [128, T])
        rstd = sb("rstd", [128, T])
        part_top = sb("part_top", [128, 8 * len(LAST_CHUNKS)])

        ident = const_sb[:, 0:128]
        tail_mask = const_sb[:, DIAGS:DIAGS + 2]

        xt_sb = q[0:C, 0, :]
        wt_sb = q[0:C, 1, 0:C]
        bias_sb = q[:, 1, C:2 * C]
        th_sb = q[:, 1, 2 * C:2 * C + 2]
        t0_diags = q[:, 2, 0:DIAGS]
        t0_diag = [q[:, 2, 0:128]] * KW + [q[:, 2, 128:128 + LAST], q[:, 2, 128 + LAST:128 + 2 * LAST]]
        diag = q[:, 2, 512:768].rearrange("p (b i) -> p b i", b=2)
        y_sb = q[:, 3, 0:T * C]

        ps = ctx.enter_context(nc.psum_tensor("ps", [128, 8 * BANK], f32))
        y_ps = ps[:, 2 * SET:2 * SET + T * C]
        unread = picked[:, :, :, :].rearrange("p s j c -> p (s j c)").bitcast(mybir.dt.bfloat16)[:, 0:N]

        y_dram = nc.dram_tensor("y_dram", [N, C], f32, kind="Internal").ap()
        vec_dram = [nc.dram_tensor(f"vec{i}_dram", [NPAD], f32, kind="Internal").ap() for i in range(3)]

        a_in = [sem(f"a_in{i}") for i in range(RING)]
        pair_in = [sem(f"pair_in{k}") for k in range(K)]
        at_in = [sem(f"at_in{i}") for i in range(2)]
        th_in, bias_in, x_in, xw_in, const_in = (
            sem("th_in"), sem("bias_in"), sem("x_in"), sem("xw_in"), sem("const_in"))
        y_mm, y_copied, y_out = sem("y_mm"), sem("y_copied"), sem("y_out")
        gate_ready, cleared, t0_ready, h_init = sem("gate_ready"), sem("cleared"), sem("t0_ready"), sem("h_init")
        rs_ready, rinv_ready, scale_ready = sem("rs_ready"), sem("rinv_ready"), sem("scale_ready")
        bh_full, bl_full, diag_sum, bh_ready, b_ready = (
            sem("bh_full"), sem("bl_full"), sem("diag_sum"), sem("bh_ready"), sem("b_ready"))
        pair_hi = [sem(f"pair_hi{r}") for r in range(2)]
        pair_lo = [sem(f"pair_lo{r}") for r in range(2)]
        masked = sem("masked")
        hi_head, hi_tail = sem("hi_head"), sem("hi_tail")
        lo_head, lo_tail = sem("lo_head"), sem("lo_tail")
        steps_done = sem("steps_done")
        degree_ready = sem("degree_ready")
        sqrt_ready, newton, vec_ready, turned, vec_out, vec_in = (
            sem("sqrt_ready"), sem("newton"), sem("vec_ready"), sem("turned"), sem("vec_out"), sem("vec_in"))
        a_used, dots_done, summed = sem("a_used"), sem("dots_done"), sem("summed")
        tile_done, evacuated, chunk_done = sem("tile_done"), sem("evacuated"), sem("chunk_done")
        scaled, diag_added, maxed, ranked, coef_ready, parts = (
            sem("scaled"), sem("diag_added"), sem("maxed"), sem("ranked"), sem("coef_ready"), sem("parts"))
        gathered = [sem(f"gathered{i}") for i in range(GS)]
        last_picked = [sem(f"last_picked{j}") for j in range(TOP)]
        mixed, h_stats, h_moments = sem("mixed"), sem("h_stats"), sem("h_moments")
        std_ready, rstd_ready, normed, stored = sem("std_ready"), sem("rstd_ready"), sem("normed"), sem("stored")

        block = ctx.enter_context(nc.Block())

        def diag_cols(k):
            cols = slice(k * 128, k * 128 + 128) if k < KW else slice(KW * 128, N)
            return cols, cols.stop - cols.start

        def ring_slot(n):
            return n % RING if n < K + T else (K + T - 1 - (n - K - T)) % RING

        def lows(k):
            return k + 1 if k < KW else k

        @block.sync
        def _(sp):
            def load_a(n):
                if n >= K + T:
                    sp.wait_ge(a_used, T + 1 + n - K - T)
                elif n >= K + RING:
                    sp.wait_ge(a_used, n - K - RING + 1)
                elif n >= RING:
                    sp.wait_ge(bl_full, n - RING + 1)
                if n >= K:
                    k = n - K if n < K + T else LOADS - 1 - n
                    src = adj[k * 128:k * 128 + rows(k), :]
                elif n >= KW:
                    src = adj_tail[(n - KW) * 128:(n - KW + 1) * 128, :]
                else:
                    src = adj[n * 128:(n + 1) * 128, :]
                s = ring_slot(n)
                sp.dma_start(a_ring[0:src.shape[0], s, :], src).then_inc(a_in[s], 16)

            def load_pair(m, k):
                if m:
                    sp.wait_ge(pair_hi[0], k + 1)
                    sp.wait_ge(pair_lo[0], lows(k))
                sp.dma_start(at_raw[:, :, k, :], adj_t[m:m + 2, :, k, :].rearrange("b p i -> p b i")
                             ).then_inc(pair_in[k], 16)

            def load_at(m):
                sp.wait_ge(lo_tail, m - 3)
                sp.dma_start(at_raw[:, m % 2, :, :], adj_t[m]).then_inc(at_in[m % 2], 16)

            def spread(i):
                sp.wait_ge(turned, i + 1)
                for g in range(4):
                    sp.dma_start(vec_dram[i].rearrange("(t g c) -> g t c", g=4, c=32)[g],
                                 in_rows[32 * g:32 * g + T, :]).then_inc(vec_out, 16)
                sp.wait_ge(vec_out, 64 * (i + 1))
                if i:
                    sp.wait_ge(dots_done, i)
                sp.dma_start(row_vec[:, :], vec_dram[i][0:N].partition_broadcast(128)).then_inc(vec_in, 16)

            for k in range(K + RING):
                load_a(k)
                if k == 0:
                    sp.dma_start(th_sb, theta.partition_broadcast(128)).then_inc(th_in, 16)
                if k < K:
                    load_pair(0, k)
                if k == 0:
                    sp.dma_start(const_sb[:, :], consts).then_inc(const_in, 16)
                if k >= RING:
                    load_pair(2, k - RING)
            spread(0)
            for n in range(K + RING, K + T):
                load_a(n)
            load_at(4)
            load_at(5)
            spread(1)
            for n in range(K + T, LOADS):
                load_a(n)
            spread(2)
            for m in range(6, T):
                load_at(m)
            sp.wait_ge(normed, T - 1)
            sp.dma_start(out[0:(T - 1) * 128, :].rearrange("(t p) c -> p t c", p=128),
                         h[:, 0:T - 1, :]).then_inc(stored, 16)
            sp.wait_ge(normed, T)
            sp.dma_start(out[(T - 1) * 128:N, :], h[0:LAST, T - 1, :]).then_inc(stored, 16)
            sp.wait_ge(stored, 32)

        @block.scalar
        def _(act):
            def row_sum(k):
                act.wait_ge(a_in[k % RING], 16 * (k // RING + 1))
                nc.scalar.activation(b_hi[:, k, :], a_ring[:, k % RING, :], ACT.Copy,
                                     accum_out=rowsum[:, k:k + 1]).then_inc(rs_ready, 1)

            act.wait_ge(th_in, 16)
            nc.scalar.activation(t_gate[:, :], th_sb, ACT.Sigmoid).then_inc(gate_ready, 1)
            row_sum(0)
            for k in range(K):
                if 0 < k < K - 1:
                    row_sum(k + 1)
                act.wait_ge(scale_ready, k + 1)
                act.wait_ge(rs_ready, k + 1)
                nc.scalar.activation(b_hi[:, k, :], a_ring[:, k % RING, :], ACT.Copy,
                                     scale=b_scale[:, k:k + 1]).then_inc(bh_full, 1)
                if k == 0:
                    row_sum(1)

            def root(i):
                act.wait_ge(vec_ready, 3 * i + 1)
                nc.scalar.activation(work[:, 0, :], rinv[:, :], ACT.Sqrt).then_inc(sqrt_ready, 1)

            root(0)

            for m in range(T - 1):
                b = m % 2
                act.wait_ge(tile_done, m + 1)
                if m == 0:
                    act.wait_ge(newton, 4)
                if m == 1:
                    act.wait_ge(h_init, 1)
                if m == 3:
                    act.wait_ge(y_out, 32)
                if m >= QS:
                    act.wait_ge(ranked, m - QS + 1)
                nc.scalar.activation(q[:, m % QS, :], ps[:, b * SET:b * SET + N], ACT.Copy,
                                     scale=d[:, m:m + 1]).then_inc(evacuated, 1)
                if m == 3:
                    root(1)
                if 4 <= m + 2 < T:
                    act.wait_ge(at_in[b], 16 * (m // 2))
                    nc.scalar.activation(at_hi[:, b, 0:HEAD, :], at_raw[:, b, 0:HEAD, :], ACT.Copy).then_inc(hi_head, 1)
                    nc.scalar.activation(at_hi[:, b, HEAD:K, :], at_raw[:, b, HEAD:K, :], ACT.Copy).then_inc(hi_tail, 1)
            act.wait_ge(h_moments, T - 1)
            nc.scalar.activation(std[:, 0:T - 1], mean_var[:, 0:T - 1, 1], ACT.Sqrt, bias=eps[:, :]).then_inc(std_ready, 1)
            act.wait_ge(h_moments, T)
            nc.scalar.activation(std[0:LAST, T - 1:T], mean_var[0:LAST, T - 1, 1:2], ACT.Sqrt,
                                 bias=eps[0:LAST, :]).then_inc(std_ready, 1)

        @block.tensor
        def _(pe):
            pe.wait_ge(xw_in, 16)
            for m in range(T):
                mm = nc.tensor.matmul(y_ps[0:rows(m), m * C:(m + 1) * C], xt_sb[:, m * 128:m * 128 + rows(m)],
                                      wt_sb, start=True, stop=True)
            mm.then_inc(y_mm, 1)

            def products(k):
                return [(at_hi, b_hi), (at_hi, b_lo), (at_lo, b_hi)] if k < KW else [(at_hi, b_hi)]

            def step(b, w, k, base, chunks=CHUNKS, follow=False):
                for n, (left, right) in enumerate(products(k)):
                    if follow and n == 1:
                        pe.wait_ge(b_ready, k + 1)
                        pe.wait_ge(pair_lo[0], k + 1)
                    for c, cw in chunks:
                        mm = nc.tensor.matmul(ps[0:w, base + c:base + c + cw], left[:, b, k, 0:w],
                                              right[:, k, c:c + cw], start=(k == 0 and n == 0), stop=(k == K - 1))
                return mm

            for k in range(K):
                pe.wait_ge(pair_hi[0], k + 1)
                if k < KW:
                    pe.wait_ge(bh_ready, k + 1)
                else:
                    pe.wait_ge(b_ready, k + 1)
                    pe.wait_ge(pair_lo[0], lows(k))
                for m in range(2):
                    mm = step(m, 128, k, m * SET, follow=(m == 0))
                    if k == K - 1:
                        mm.then_inc(tile_done, 1)
                    elif m == 1:
                        mm.then_inc(steps_done, 1)

            with pe.Fori(0, (T - 3) // 2) as i:
                for b in range(2):
                    pe.wait_ge(evacuated, 2 * i + (b + 1))
                    for k in range(K):
                        if k == 0:
                            pe.wait_ge(lo_head, 2 * i + (b + 1))
                        if k == HEAD:
                            pe.wait_ge(lo_tail, 2 * i + (b + 1))
                        mm = step(b, 128, k, b * SET)
                    mm.then_inc(tile_done, 1)

            pe.wait_ge(evacuated, T - 2)
            pe.wait_ge(lo_tail, T - 2)
            for n, (c, cw) in enumerate(LAST_CHUNKS):
                for k in range(K):
                    mm = step(0, LAST, k, n * BANK - c, [(c, cw)])
                mm.then_inc(chunk_done, 1)

        @block.vector
        def _(dve):
            nc.vector.memset(eps[:, :], EPS)
            nc.vector.memset(dot[:, :], 1.0)
            nc.vector.memset(to_rows[:, :], 0.0).then_inc(cleared, 1)

            def inverse_of(k):
                dve.wait_ge(rs_ready, k + 1)
                nc.vector.reciprocal(rinv_k[:, k:k + 1], rowsum[:, k:k + 1]).then_inc(rinv_ready, 1)

            def scale_of(k):
                dve.wait_ge(rinv_ready, k + 1)
                nc.vector.tensor_tensor(b_scale[:, k:k + 1], rinv_k[:, k:k + 1], t_gate[:, 1:2],
                                        ALU.mult).then_inc(scale_ready, 1)

            def pair_high(r, k):
                dve.wait_ge(pair_in[k], 16 * (r + 1))
                if r:
                    if k < K - 1:
                        dve.wait_ge(steps_done, k + 1)
                    else:
                        dve.wait_ge(tile_done, 2)
                nc.vector.tensor_copy(at_hi[:, :, k, :], at_raw[:, :, k, :]).then_inc(pair_hi[r], 1)

            def diagonal(k):
                cols, w = diag_cols(k)
                dve.wait_ge(scale_ready, k + 1)
                if k >= 2:
                    dve.wait_ge(b_ready, k - 1)
                nc.vector.scalar_tensor_tensor(diag[:, k % 2, 0:w], a_ring[:, k % RING, cols], b_scale[:, k:k + 1],
                                               t0_diag[k], ALU.mult, ALU.add).then_inc(diag_sum, 1)

            def diagonal_high(k):
                cols, w = diag_cols(k)
                dve.wait_ge(diag_sum, k + 1)
                nc.vector.tensor_copy(b_hi[:, k, cols], diag[:, k % 2, 0:w]).then_inc(bh_ready, 1)

            inverse_of(0)
            dve.wait_ge(const_in, 16)
            dve.wait_ge(gate_ready, 1)
            nc.vector.tensor_scalar(t0_diags, const_sb[:, 0:DIAGS], t_gate[:, 0:1], None, ALU.mult).then_inc(t0_ready, 1)
            scale_of(0)
            pair_high(0, 0)
            dve.wait_ge(t0_ready, 1)
            diagonal(0)
            for k in range(K):
                cols, w = diag_cols(k)
                p = slice(LO_FROM.get(k, 0), 128)
                if 0 < k < K - 1:
                    inverse_of(k + 1)
                dve.wait_ge(bh_full, k + 1)
                if k < KW:
                    diagonal_high(k)
                if 0 < k < K - 1:
                    scale_of(k + 1)
                if k < KW:
                    dve.wait_ge(bh_ready, k + 1)
                lo = b_lo[:, k, :] if k < KW else b_hi[LO_FROM[k]:, k, :]
                nc.vector.scalar_tensor_tensor(lo, a_ring[p, k % RING, :], b_scale[p, k:k + 1],
                                               b_hi[p, k, :].bitcast(f32), ALU.mult, ALU.subtract).then_inc(bl_full, 1)
                if k == 0:
                    inverse_of(1)
                    pair_high(0, 1)
                    scale_of(1)
                elif k + 1 < K:
                    pair_high(0, k + 1)
                dve.wait_ge(bl_full, k + 1)
                if k >= KW:
                    diagonal_high(k)
                if k + 1 < K:
                    diagonal(k + 1)
                dve.wait_ge(bh_ready, k + 1)
                lo = b_lo[:, k, cols] if k < KW else b_hi[p, k, cols]
                nc.vector.tensor_tensor(lo, diag[p, k % 2, 0:w], b_hi[p, k, cols].bitcast(f32),
                                        ALU.subtract).then_inc(b_ready, 1)
                if k == 1:
                    dve.wait_ge(y_mm, 1)
                    nc.vector.tensor_copy(y_sb[:, 0:(T - 1) * C], y_ps[:, 0:(T - 1) * C])
                    nc.vector.tensor_copy(y_sb[0:LAST, (T - 1) * C:], y_ps[0:LAST, (T - 1) * C:]).then_inc(y_copied, 1)
                if k >= RING:
                    pair_high(1, k - RING)

            nc.vector.tensor_copy(degree[:, :], rowsum[:, 0:T]).then_inc(degree_ready, 1)
            dve.wait_ge(degree_ready, 1)
            nc.vector.tensor_copy(degree[64:LAST, T - 1:T], rowsum[64:LAST, Y:Y + 1]).then_inc(degree_ready, 1)
            dve.wait_ge(degree_ready, 2)

            def inverse_root(i, degrees, result):
                nc.vector.reciprocal(rinv[:, :], degrees).then_inc(vec_ready, 1)
                dve.wait_ge(sqrt_ready, i + 1)
                nc.vector.tensor_tensor(work[:, 1, :], work[:, 0, :], work[:, 0, :], ALU.mult).then_inc(newton, 1)
                dve.wait_ge(newton, 4 * i + 1)
                nc.vector.tensor_tensor(work[:, 2, :], work[:, 1, :], degrees, ALU.mult).then_inc(newton, 1)
                dve.wait_ge(newton, 4 * i + 2)
                nc.vector.tensor_scalar(work[:, 3, :], work[:, 2, :], -0.5, 1.5, ALU.mult, ALU.add).then_inc(newton, 1)
                dve.wait_ge(newton, 4 * i + 3)
                nc.vector.tensor_tensor(result, work[:, 3, :], work[:, 0, :], ALU.mult).then_inc(newton, 1)
                dve.wait_ge(newton, 4 * i + 4)

            def turn(i, vector_copied):
                vector_copied.then_inc(vec_ready, 1)
                dve.wait_ge(vec_ready, [2, 3, 5][i])
                if i:
                    dve.wait_ge(vec_out, 64 * i)
                nc.vector.transpose(in_rows[:, :], to_rows[:, :]).then_inc(turned, 1)

            def dots(i):
                dve.wait_ge(vec_in, 16 * (i + 1))
                for k in range(T):
                    if i == 0:
                        n, t = K + k, k
                    else:
                        n, t = (K + T - 1 - k if k < RING else K + T + k - RING), T - 1 - k
                    p = rows(t)
                    s = ring_slot(n)
                    dve.wait_ge(a_in[s], 16 * sum(ring_slot(j) == s for j in range(n + 1)))
                    if k or i:
                        dve.wait_ge(a_used, T * i + k)
                    nc.vector.scalar_tensor_tensor(unread[0:p, :], a_ring[0:p, s, :], 1.0,
                                                   row_vec[0:p, :], ALU.mult, ALU.mult,
                                                   accum_out=dot[0:p, t:t + 1]).then_inc(a_used, 1)
                dve.wait_ge(a_used, T * (i + 1))

            dve.wait_ge(cleared, 1)
            inverse_root(0, degree[:, :], d[:, :])
            turn(0, nc.vector.tensor_copy(to_rows[:, 0:T], d[:, :]))

            dve.wait_ge(x_in, 32)
            dve.wait_ge(bias_in, 16)
            nc.vector.tensor_tensor(h[:, 0:T - 1, :], h[:, 0:T - 1, :],
                                    bias_sb.unsqueeze(1).broadcast_to([128, T - 1, C]), ALU.add)
            nc.vector.tensor_tensor(h[0:LAST, T - 1, :], h[0:LAST, T - 1, :], bias_sb[0:LAST, :],
                                    ALU.add).then_inc(h_init, 1)

            for k in range(K - RING, K):
                pair_high(1, k)

            dots(0)
            nc.vector.tensor_tensor(u[:, :], dot[:, :], rinv[:, :], ALU.mult).then_inc(dots_done, 1)
            dve.wait_ge(dots_done, 1)
            nc.vector.tensor_scalar(work[:, 1, :], u[:, :], t_gate[:, 1:2], None, ALU.mult).then_inc(summed, 1)
            dve.wait_ge(summed, 1)
            turn(1, nc.vector.scalar_tensor_tensor(to_rows[:, 0:T], d[:, :], t_gate[:, 0:1], work[:, 1, :],
                                                   ALU.mult, ALU.add))

            dots(1)
            nc.vector.tensor_tensor(deg2[:, :], dot[:, :], d[:, :], ALU.mult).then_inc(dots_done, 1)
            dve.wait_ge(dots_done, 2)
            nc.vector.tensor_scalar(deg2[:, :], deg2[:, :], 1.0, None, ALU.add).then_inc(summed, 1)
            dve.wait_ge(summed, 2)
            inverse_root(1, deg2[:, :], e[:, :])
            turn(2, nc.vector.tensor_tensor(to_rows[:, 0:T], d[:, :], e[:, :], ALU.mult))
            dve.wait_ge(vec_in, 48)

            def add_diagonal(m, after):
                p = rows(m)
                mm = slice(m * 128, m * 128 + p)
                dve.wait_ge(scaled, after)
                nc.vector.scalar_tensor_tensor(q[0:p, m % QS, mm], ident[0:p, 0:p], e[0:p, m:m + 1],
                                               q[0:p, m % QS, mm], ALU.mult, ALU.add).then_inc(diag_added, 1)
                dve.wait_ge(diag_added, m + 1)

            def locate(m):
                p = rows(m)
                dve.wait_ge(maxed, m + 1)
                nc.vector.max_index(top_at[0:p, m, :], top[0:p, m, :], q[0:p, m % QS, :]).then_inc(ranked, 1)
                nc.vector.tensor_scalar(coef[0:p, m, :], top[0:p, m, 0:TOP], e[0:p, m:m + 1], None,
                                        ALU.mult).then_inc(coef_ready, 1)

            def rank(m):
                s = q[:, m % QS, :]
                dve.wait_ge(evacuated, m + 1)
                nc.vector.tensor_tensor(s, s, row_vec[:, :], ALU.mult).then_inc(scaled, 1)
                add_diagonal(m, m + 1)
                nc.vector.max(top[:, m, :], s).then_inc(maxed, 1)
                locate(m)

            def rank_part(n):
                m, p = T - 1, LAST
                c, cw = LAST_CHUNKS[n]
                s = q[0:p, m % QS, c:c + cw]
                dve.wait_ge(chunk_done, n + 1)
                nc.vector.scalar_tensor_tensor(s, ps[0:p, n * BANK:n * BANK + cw], d[0:p, m:m + 1],
                                               row_vec[0:p, c:c + cw], ALU.mult, ALU.mult).then_inc(scaled, 1)
                if n == 0:
                    add_diagonal(m, m + 1)
                else:
                    dve.wait_ge(scaled, m + 1 + n)
                nc.vector.max(part_top[0:p, 8 * n:8 * n + 8], s).then_inc(parts, 1)

            def rank_last():
                m, p = T - 1, LAST
                dve.wait_ge(parts, len(LAST_CHUNKS))
                nc.vector.max(top[0:p, m, :], part_top[0:p, :]).then_inc(maxed, 1)
                locate(m)

            def mix(m):
                p = rows(m)
                if m < T - 1:
                    dve.wait_ge(gathered[m % GS], 16 * TOP * (m // GS + 1))
                dve.wait_ge(coef_ready, m + 1)
                for j in range(TOP):
                    if m == T - 1:
                        dve.wait_ge(last_picked[j], 16)
                    if j:
                        dve.wait_ge(mixed, TOP * m + j)
                    nc.vector.scalar_tensor_tensor(h[0:p, m, :], picked[0:p, m % GS, j, :], coef[0:p, m, j:j + 1],
                                                   h[0:p, m, :], ALU.mult, ALU.add).then_inc(mixed, 1)
                dve.wait_ge(mixed, TOP * (m + 1))
                if m:
                    dve.wait_ge(h_moments, m)
                nc.vector.bn_stats(stats[0:p, :], h[0:p, m, :]).then_inc(h_stats, 1)
                dve.wait_ge(h_stats, m + 1)
                nc.vector.bn_aggr(mean_var[0:p, m, :], stats[0:p, :]).then_inc(h_moments, 1)

            def normalise(i, lo, hi):
                p = rows(hi - 1)
                dve.wait_ge(std_ready, i + 1)
                nc.vector.reciprocal(rstd[0:p, lo:hi], std[0:p, lo:hi]).then_inc(rstd_ready, 1)
                dve.wait_ge(rstd_ready, i + 1)
                for m in range(lo, hi):
                    nc.vector.tensor_scalar(h[0:p, m, :], h[0:p, m, :], mean_var[0:p, m, 0:1], rstd[0:p, m:m + 1],
                                            ALU.subtract, ALU.mult).then_inc(normed, 1)

            for i in range((T - 1) // 2):
                rank(2 * i)
                rank(2 * i + 1)
                if i:
                    mix(2 * i - 2)
                    mix(2 * i - 1)
            rank_part(0)
            mix(T - 3)
            mix(T - 2)
            rank_part(1)
            normalise(0, 0, T - 1)
            rank_part(2)
            rank_last()
            mix(T - 1)
            normalise(1, T - 1, T)

        @block.gpsimd
        def _(pool):
            def masked_y(y_raw, y_half, ready, count):
                pool.tensor_scalar(y_raw, y_raw, tail_mask[:, 1:2], None, ALU.mult).then_inc(masked, 1)
                pool.tensor_scalar(y_half, y_half.bitcast(f32), tail_mask[:, 0:1], None, ALU.mult).then_inc(masked, 1)
                pool.wait_ge(masked, 2 * count)
                pool.tensor_tensor(y_half, y_half.bitcast(f32), y_raw, ALU.add).then_inc(*ready)

            def pair_low(r, k):
                if k == X:
                    return
                pool.wait_ge(pair_hi[r], k + 1)
                ready = (lo_head, 2) if r and k == HEAD - 1 else (lo_tail, 2) if r and k == Y else (pair_lo[r], 1)
                if k < KW:
                    pool.tensor_tensor(at_lo[:, :, k, :], at_raw[:, :, k, :], at_hi[:, :, k, :].bitcast(f32),
                                       ALU.subtract).then_inc(*ready)
                else:
                    masked_y(at_raw[:, :, Y, :], at_hi[:, :, Y, :], ready, r + 1)

            def low_half(m):
                b = m % 2
                pool.wait_ge(hi_head, m - 3)
                pool.tensor_tensor(at_lo[:, b, 0:HEAD, :], at_raw[:, b, 0:HEAD, :],
                                   at_hi[:, b, 0:HEAD, :].bitcast(f32), ALU.subtract).then_inc(lo_head, 1)
                pool.wait_ge(hi_tail, m - 3)
                pool.tensor_tensor(at_lo[:, b, HEAD:KW, :], at_raw[:, b, HEAD:KW, :],
                                   at_hi[:, b, HEAD:KW, :].bitcast(f32), ALU.subtract)
                masked_y(at_raw[:, b, Y, :], at_hi[:, b, Y, :], (lo_tail, 1), m - 1)

            def gather(m):
                p = rows(m)
                pool.wait_ge(ranked, m + 1)
                if m >= GS:
                    pool.wait_ge(mixed, TOP * (m - GS + 1))
                for j in range(TOP):
                    pool.indirect_dma_start(picked[0:p, m % GS, j, :], None, y_dram,
                                            bass.IndirectOffsetOnAxis(top_at[0:p, m, j:j + 1], 0)
                                            ).then_inc(gathered[m % GS] if m < T - 1 else last_picked[j], 16)

            pool.dma_start(q[0:C, 0:2, :].rearrange("p s n -> p (s n)")[:, 0:N + C], xw_t).then_inc(xw_in, 16)
            pool.wait_ge(const_in, 16)
            for k in range(K):
                pair_low(0, k)
                if k == K - 3:
                    pool.dma_start(bias_sb, bias.partition_broadcast(128)).then_inc(bias_in, 16)
                    pool.dma_start(h[:, 0:T - 1, :], x[0:(T - 1) * 128, :].rearrange("(t p) c -> p t c", p=128)
                                   ).then_inc(x_in, 16)
                    pool.dma_start(h[0:LAST, T - 1, :], x[(T - 1) * 128:N, :]).then_inc(x_in, 16)
                if k == K - 1:
                    pool.wait_ge(y_copied, 1)
                    pool.dma_start(y_dram[0:(T - 1) * 128, :].rearrange("(t p) c -> p t c", p=128),
                                   y_sb[:, 0:(T - 1) * C].rearrange("p (t c) -> p t c", c=C)).then_inc(y_out, 16)
                    pool.dma_start(y_dram[(T - 1) * 128:N, :], y_sb[0:LAST, (T - 1) * C:]).then_inc(y_out, 16)
                if k >= RING:
                    pair_low(1, k - RING)
            for k in range(K - RING, K):
                pair_low(1, k)
            low_half(4)
            low_half(5)
            pool.wait_ge(y_out, 32)
            for i in range((T - 1) // 2):
                low_half(i + 6)
                gather(2 * i)
                gather(2 * i + 1)
            gather(T - 1)


def _tail_rows(n):
    import numpy as _np
    whole = n // 128 * 128
    rest = _np.arange(whole + 64, n)
    first = _np.arange(whole, whole + 64)
    mask = _np.zeros((128, 2), _np.float32)
    mask[0:64] = -1, 1
    y = _np.full(128, whole)
    y[0:64] = first
    at = 64
    for at, kind in ((64, (1, 0)), (64 + len(rest), (-1, 1)), (96, (1, 0))):
        y[at:at + len(rest)] = rest
        mask[at:at + len(rest)] = kind
    return _np.concatenate([first, first, y]), mask


_SHAPE = (1354, 64)


def kernel(**inputs):
    import numpy as _np
    import concourse.bacc as _bacc
    from concourse import mybir as _mybir
    from concourse.bass_utils import run_bass_kernel_spmd as _run

    nc = _bacc.Bacc("TRN2", target_bir_lowering=False, num_devices=1)
    adj = _np.asarray(inputs["adj"])
    n = adj.shape[0]
    whole, tiles = n // 128, (n + 127) // 128
    tail, mask = _tail_rows(n)
    adj_t = _np.zeros((tiles, 128, whole + 2, 128), adj.dtype)
    steps = _np.concatenate([_np.arange(whole * 128), tail]).reshape(whole + 2, 128)
    for m in range(tiles):
        part = adj[m * 128:(m + 1) * 128]
        adj_t[m, :, :, 0:part.shape[0]] = part.T[steps].transpose(1, 0, 2)
    ones = _np.zeros((128, 128 + 2 * (n - whole * 128)), _np.float32)
    ones[:, 0:128] = _np.eye(128)
    for s in range(2):
        for p in range(128):
            ones[p, 128 + s * (n - whole * 128) + tail[s * 128 + p] - whole * 128] = 1
    laid_out = {
        "x": inputs["x"], "adj": adj, "adj_tail": adj[tail], "adj_t": adj_t, "xw_t": _np.concatenate([_np.asarray(inputs["x"]).T, _np.asarray(inputs["L0_gnn_W"]).T], axis=1),
        "theta": inputs["L0_gnn_theta"], "bias": inputs["L0_gnn_b"],
        "consts": _np.concatenate([ones, mask], axis=1),
    }
    arrays, args = {}, []
    for name, a in laid_out.items():
        a = _np.ascontiguousarray(a)
        arrays[f"in_{name}"] = a
        args.append(nc.dram_tensor(f"in_{name}", a.shape, _mybir.dt.from_np(a.dtype), kind="ExternalInput").ap())
    args.append(nc.dram_tensor("out_0", _SHAPE, _mybir.dt.float32, kind="ExternalOutput").ap())
    program(nc, *args)
    r = _run(nc, [arrays], core_ids=[0])
    return r.results[0]["out_0"]
```
